# Optimizing a Trainium2 kernel written in Bass

```python
import numpy as np
import jax
import jax.numpy as jnp

def _softmax(x, axis=-1):
    return jax.nn.softmax(x, axis=axis)

def _gelu(x):
    return jax.nn.gelu(x, approximate=True)

def _silu(x):
    return jax.nn.silu(x)

def _sigmoid(x):
    return jax.nn.sigmoid(x)

def _layernorm(x, axis=-1, eps=1e-05):
    m = jnp.mean(x, axis=axis, keepdims=True)
    v = jnp.var(x, axis=axis, keepdims=True)
    return (x - m) / jnp.sqrt(v + eps)

def _scatter_add(tgt, idx, src, axis=0):
    return tgt.at[idx].add(src)

def _segment_sum(src, seg, n):
    return jax.ops.segment_sum(src, seg, n)
kernel_name = 'mk_gnn_preln_d4_gnn_r8_bd3655'

def setup_inputs(seed: int=0):
    np.random.seed(seed)
    _w = jnp.asarray

    def _rec_inputs():
        import jax
        import jax.numpy as jnp
        _gk = jax.random.key(seed)
        x = -0.000202 + 1 * jax.random.normal(jax.random.fold_in(_gk, 1), (12500, 64), jnp.float32)
        _s = jax.random.randint(jax.random.fold_in(_gk, 2), (100000,), 0, 12500, jnp.int32)
        _d = jax.random.randint(jax.random.fold_in(_gk, 3), (100000,), 0, 12500, jnp.int32)
        _loop = jnp.arange(12500, dtype=jnp.int32)
        src = jnp.concatenate([_s, _d, _loop])
        dst = jnp.concatenate([_d, _s, _loop])
        _o = jnp.argsort(dst, stable=True)
        src = src[_o]
        dst = dst[_o]
        edge_attr_32 = 0.000102155 + 1.00015 * jax.random.normal(jax.random.fold_in(_gk, 12), (212500, 32), jnp.float32)
        edge_type_200 = jax.random.randint(jax.random.fold_in(_gk, 14), (212500,), 0, 200, jnp.int32)
        return (x, src, dst, edge_attr_32, edge_type_200)
    x, src, dst, edge_attr_32, edge_type_200 = _rec_inputs()

    def _L0_gnn_setup():
        import jax, jax.numpy as jnp
        import numpy as np
        N_ENT = 12500
        N_REL = 200
        D = 64
        E = 150000

        def _edge_norm(edge_index, num_ent):
            row, col = (edge_index[0], edge_index[1])
            ones = jnp.ones(row.shape[0], dtype=jnp.float32)
            deg = jax.ops.segment_sum(ones, row, num_segments=num_ent)
            deg_inv = jnp.where(deg > 0, jax.lax.rsqrt(jnp.maximum(deg, 1.0)), 0.0)
            return deg_inv[row] * deg_inv[col]
        key = jax.random.key(seed)
        k1, k2, k3, k4, k5 = jax.random.split(key, 5)
        x = jax.random.normal(k1, (N_ENT, D), dtype=jnp.float32)
        r = jax.random.normal(k2, (N_REL, D), dtype=jnp.float32)
        W = jax.random.normal(k3, (D, D), dtype=jnp.float32) * (1.0 / np.sqrt(D))
        edge_index = jax.random.randint(k4, (2, E), 0, N_ENT, dtype=jnp.int64)
        edge_type = jax.random.randint(k5, (E,), 0, N_REL, dtype=jnp.int64)
        return {'x': x, 'r': r, 'W': W, 'edge_index': edge_index, 'edge_type': edge_type}
    _L0_gnn_all = _L0_gnn_setup()
    _L0_gnn_in = {k: v for k, v in _L0_gnn_all.items() if k in ('r', 'W')}
    del _L0_gnn_all

    def _L1_gnn_setup():
        import jax, jax.numpy as jnp
        import numpy as np
        N_NODES = 12500
        N_EDGES = 125000
        NODE_DIM = 64
        EDGE_DIM = 32
        HIDDEN = 64

        def _unif(key, shape, fan_in):
            bound = 1.0 / np.sqrt(fan_in)
            return jax.random.uniform(key, shape, jnp.float32, -bound, bound)
        key = jax.random.key(seed)
        ks = jax.random.split(key, 11)
        node_features = jax.random.normal(ks[0], (N_NODES, NODE_DIM), jnp.float32)
        edge_index = jax.random.randint(ks[1], (2, N_EDGES), 0, N_NODES, dtype=jnp.int64)
        edge_features = jax.random.normal(ks[2], (N_EDGES, EDGE_DIM), jnp.float32)
        in_dim = 2 * NODE_DIM + EDGE_DIM
        W1 = _unif(ks[3], (HIDDEN, in_dim), in_dim)
        b1 = _unif(ks[4], (HIDDEN,), in_dim)
        W2 = _unif(ks[5], (HIDDEN, HIDDEN), HIDDEN)
        b2 = _unif(ks[6], (HIDDEN,), HIDDEN)
        w_ih = _unif(ks[7], (3 * NODE_DIM, HIDDEN), NODE_DIM)
        w_hh = _unif(ks[8], (3 * NODE_DIM, NODE_DIM), NODE_DIM)
        b_ih = _unif(ks[9], (3 * NODE_DIM,), NODE_DIM)
        b_hh = _unif(ks[10], (3 * NODE_DIM,), NODE_DIM)
        return {'node_features': node_features, 'edge_index': edge_index, 'edge_features': edge_features, 'W1': W1, 'b1': b1, 'W2': W2, 'b2': b2, 'w_ih': w_ih, 'w_hh': w_hh, 'b_ih': b_ih, 'b_hh': b_hh}
    _L1_gnn_all = _L1_gnn_setup()
    _L1_gnn_in = {k: v for k, v in _L1_gnn_all.items() if k in ('W1', 'b1', 'W2', 'b2', 'w_ih', 'w_hh', 'b_ih', 'b_hh')}
    del _L1_gnn_all

    def _L2_gnn_setup():
        import jax, jax.numpy as jnp
        import numpy as np
        N_NODES = 12500
        N_EDGES = 200000
        D = 64
        H = 128
        key = jax.random.key(seed)
        k = jax.random.split(key, 8)
        feat = jax.random.normal(k[0], (N_NODES, D), dtype=jnp.float32)
        edge_src = jax.random.randint(k[1], (N_EDGES,), 0, N_NODES, dtype=jnp.int32)
        edge_dst = jax.random.randint(k[2], (N_EDGES,), 0, N_NODES, dtype=jnp.int32)
        W1 = jax.random.normal(k[3], (D, H), dtype=jnp.float32) * (1.0 / np.sqrt(D))
        b1 = jnp.zeros((H,), dtype=jnp.float32)
        W2 = jax.random.normal(k[4], (H, D), dtype=jnp.float32) * (1.0 / np.sqrt(H))
        b2 = jnp.zeros((D,), dtype=jnp.float32)
        eps = jnp.zeros((1,), dtype=jnp.float32)
        return {'feat': feat, 'edge_src': edge_src, 'edge_dst': edge_dst, 'W1': W1, 'b1': b1, 'W2': W2, 'b2': b2, 'eps': eps}
    _L2_gnn_all = _L2_gnn_setup()
    _L2_gnn_in = {k: v for k, v in _L2_gnn_all.items() if k in ('W1', 'b1', 'W2', 'b2', 'eps')}
    del _L2_gnn_all

    def _L3_gnn_setup():
        import jax, jax.numpy as jnp
        import numpy as np
        N_NODES = 12500
        key = jax.random.key(seed)
        k1, k2, k3, k4, k5 = jax.random.split(key, 5)
        x = jax.random.normal(k1, (N_NODES, 64), dtype=jnp.float32)
        edge_index = jax.random.randint(k2, (2, 200000), 0, N_NODES, dtype=jnp.int32)
        W_l = jax.random.normal(k3, (64, 64), dtype=jnp.float32) * 0.1
        b_l = jax.random.normal(k4, (64,), dtype=jnp.float32) * 0.1
        W_r = jax.random.normal(k5, (64, 64), dtype=jnp.float32) * 0.1
        return {'x': x, 'edge_index': edge_index, 'W_l': W_l, 'b_l': b_l, 'W_r': W_r}
    _L3_gnn_all = _L3_gnn_setup()
    _L3_gnn_in = {k: v for k, v in _L3_gnn_all.items() if k in ('W_l', 'b_l', 'W_r')}
    del _L3_gnn_all
    return {'x': x, 'src': src, 'dst': dst, 'edge_attr_32': edge_attr_32, 'edge_type_200': edge_type_200, 'L0_gnn_r': _L0_gnn_in['r'], 'L0_gnn_W': _L0_gnn_in['W'], 'L1_gnn_W1': _L1_gnn_in['W1'], 'L1_gnn_b1': _L1_gnn_in['b1'], 'L1_gnn_W2': _L1_gnn_in['W2'], 'L1_gnn_b2': _L1_gnn_in['b2'], 'L1_gnn_w_ih': _L1_gnn_in['w_ih'], 'L1_gnn_w_hh': _L1_gnn_in['w_hh'], 'L1_gnn_b_ih': _L1_gnn_in['b_ih'], 'L1_gnn_b_hh': _L1_gnn_in['b_hh'], 'L2_gnn_W1': _L2_gnn_in['W1'], 'L2_gnn_b1': _L2_gnn_in['b1'], 'L2_gnn_W2': _L2_gnn_in['W2'], 'L2_gnn_b2': _L2_gnn_in['b2'], 'L2_gnn_eps': _L2_gnn_in['eps'], 'L3_gnn_W_l': _L3_gnn_in['W_l'], 'L3_gnn_b_l': _L3_gnn_in['b_l'], 'L3_gnn_W_r': _L3_gnn_in['W_r']}

def reference(x, src, dst, edge_attr_32, edge_type_200, L0_gnn_r, L0_gnn_W, L1_gnn_W1, L1_gnn_b1, L1_gnn_W2, L1_gnn_b2, L1_gnn_w_ih, L1_gnn_w_hh, L1_gnn_b_ih, L1_gnn_b_hh, L2_gnn_W1, L2_gnn_b1, L2_gnn_W2, L2_gnn_b2, L2_gnn_eps, L3_gnn_W_l, L3_gnn_b_l, L3_gnn_W_r):
    import jax
    import jax.numpy as jnp

    def _L0_gnn_ref(x, r, W, edge_index, edge_type):
        import jax, jax.numpy as jnp
        import numpy as np
        N_ENT = 12500
        N_REL = 200
        D = 64
        E = 150000

        def _edge_norm(edge_index, num_ent):
            row, col = (edge_index[0], edge_index[1])
            ones = jnp.ones(row.shape[0], dtype=jnp.float32)
            deg = jax.ops.segment_sum(ones, row, num_segments=num_ent)
            deg_inv = jnp.where(deg > 0, jax.lax.rsqrt(jnp.maximum(deg, 1.0)), 0.0)
            return deg_inv[row] * deg_inv[col]
        h_j = x[edge_index[1]]
        h_r = r[edge_type]
        composed = h_j
        msg = composed @ W
        norm = _edge_norm(edge_index, N_ENT)
        msg = msg * norm[:, None]
        out = jax.ops.segment_sum(msg, edge_index[0], num_segments=N_ENT)
        return out

    def _L1_gnn_ref(node_features, edge_index, edge_features, W1, b1, W2, b2, w_ih, w_hh, b_ih, b_hh):
        import jax, jax.numpy as jnp
        import numpy as np
        N_NODES = 12500
        N_EDGES = 125000
        NODE_DIM = 64
        EDGE_DIM = 32
        HIDDEN = 64

        def _unif(key, shape, fan_in):
            bound = 1.0 / np.sqrt(fan_in)
            return jax.random.uniform(key, shape, jnp.float32, -bound, bound)
        src, dst = (edge_index[0], edge_index[1])
        x = jnp.concatenate([node_features[src], node_features[dst], edge_features], axis=-1)
        h = jax.nn.relu(x @ W1.T + b1)
        messages = h @ W2.T + b2
        agg = jax.ops.segment_sum(messages, dst, num_segments=node_features.shape[0])
        gi = agg @ w_ih.T + b_ih
        gh = node_features @ w_hh.T + b_hh
        i_r, i_z, i_n = jnp.split(gi, 3, axis=-1)
        h_r, h_z, h_n = jnp.split(gh, 3, axis=-1)
        r = jax.nn.sigmoid(i_r + h_r)
        z = jax.nn.sigmoid(i_z + h_z)
        n = jnp.tanh(i_n + r * h_n)
        return (1.0 - z) * n + z * node_features

    def _L2_gnn_ref(feat, edge_src, edge_dst, W1, b1, W2, b2, eps):
        import jax, jax.numpy as jnp
        import numpy as np
        N_NODES = 12500
        N_EDGES = 200000
        D = 64
        H = 128
        neigh = jax.ops.segment_sum(feat[edge_src], edge_dst, num_segments=N_NODES)
        h = (1.0 + eps[0]) * feat + neigh
        h = jnp.maximum(h @ W1 + b1, 0.0) @ W2 + b2
        return h

    def _L3_gnn_ref(x, edge_index, W_l, b_l, W_r):
        import jax, jax.numpy as jnp
        import numpy as np
        N_NODES = 12500
        src = edge_index[0]
        dst = edge_index[1]
        msg = x[src]
        agg = jax.ops.segment_sum(msg, dst, num_segments=N_NODES)
        cnt = jax.ops.segment_sum(jnp.ones_like(dst, dtype=x.dtype), dst, num_segments=N_NODES)
        mean = agg / jnp.maximum(cnt, 1.0)[:, None]
        out = mean @ W_l.T + b_l + x @ W_r.T
        return jax.nn.relu(out)
    edge_index = jnp.stack([src, dst])
    h = jnp.maximum(_layernorm(x, axis=-1), 0.0)
    x = x + _L0_gnn_ref(h, L0_gnn_r, L0_gnn_W, edge_index, edge_type_200)
    h = jnp.maximum(_layernorm(x, axis=-1), 0.0)
    x = x + _L1_gnn_ref(h, edge_index, edge_attr_32, L1_gnn_W1, L1_gnn_b1, L1_gnn_W2, L1_gnn_b2, L1_gnn_w_ih, L1_gnn_w_hh, L1_gnn_b_ih, L1_gnn_b_hh)
    h = jnp.maximum(_layernorm(x, axis=-1), 0.0)
    x = x + _L2_gnn_ref(h, src, dst, L2_gnn_W1, L2_gnn_b1, L2_gnn_W2, L2_gnn_b2, L2_gnn_eps)
    h = jnp.maximum(_layernorm(x, axis=-1), 0.0)
    x = x + _L3_gnn_ref(h, edge_index, L3_gnn_W_l, L3_gnn_b_l, L3_gnn_W_r)
    return x

_drawn_inputs = setup_inputs


def setup_inputs(seed=0):
    import zlib

    import numpy as np

    out = dict(_drawn_inputs(seed))
    spreads = {'L2_gnn_b1': (0.0, 0.616), 'L2_gnn_b2': (0.0, 0.425)}
    factors = {'L1_gnn_b_hh': 3.662, 'L3_gnn_b_l': 2.973}
    for name, (base, spread) in spreads.items():
        noise = np.random.default_rng([zlib.crc32(name.encode()), seed]).standard_normal(out[name].shape)
        drawn = base * np.exp(spread * noise) if base else spread * noise
        out[name] = jnp.asarray(drawn.astype(out[name].dtype))
    for name, factor in factors.items():
        out[name] = (out[name] * factor).astype(out[name].dtype)
    return out
```

```python
from contextlib import ExitStack

import concourse.bass as bass
from concourse import mybir

ALU = mybir.AluOpType
ACT = mybir.ActivationFunctionType
AX_X = mybir.AxisListType.X
F32 = mybir.dt.float32
BF16 = mybir.dt.bfloat16
I32 = mybir.dt.int32

P = 128
N_NODES = 12500
N_EDGES = 212500
F = 64
EDGE_F = 32
HID = 128
J = 104
NP = J * P
JG = 4
GN = JG * P
GROUPS = J // JG
CHUNKS = 4
JC = J // CHUNKS
K = 8
ST = K * P
SUPERS = -(-N_EDGES // ST)
SUPERS += SUPERS % 2
HALF = SUPERS // 2
TILES = SUPERS * K
EP = TILES * P
PAD_NODE = N_NODES
PARTS = 4
PACK = P
BASE_MAX = NP - P
EPS = 1e-5
ROUND = 16 * HALF

assert GROUPS % 2 == 0 and J % CHUNKS == 0 and PAD_NODE + P <= NP <= PACK * P and HALF <= P


def need(eng, sem, value):
    if not (isinstance(value, int) and value <= 0):
        eng.wait_ge(sem, value)


def first_then_loop(eng, n):
    yield 0
    with eng.Fori(1, n) as i:
        yield i


def gnn_kernel(nc, x_in, src_steps, src_cols, dst_cols, edge_t, w0bd, w1ab, w1c, w2b, wgate, bih, bhh,
               w21, b21, w22, b22, eps_in, wl3, wr3b, out):
    with ExitStack() as ctx:
        def sb(c, name, shape, dt=F32):
            return c.enter_context(nc.sbuf_tensor(name, shape, dt))

        def psum(c, name, shape, dt=F32):
            return c.enter_context(nc.psum_tensor(name, shape, dt))

        def lasting_sem(name):
            return ctx.enter_context(nc.semaphore(name))

        stage_sems = []

        def sem(name):
            stage_sems.append(nc.alloc_semaphore(name=name))
            return stage_sems[-1]

        def end_stage():
            nc.clear_and_free_semaphores(stage_sems)
            nc.all_engine_barrier()
            stage_sems.clear()

        u_tab = nc.dram_tensor("u_tab", [NP, F], F32).ap()
        a_tab = nc.dram_tensor("a_tab", [NP, F], F32).ap()
        b_tab = nc.dram_tensor("b_tab", [NP, F], F32).ap()
        h2_tab = nc.dram_tensor("h2_tab", [NP, F], F32).ap()
        h3_tab = nc.dram_tensor("h3_tab", [NP, F], F32).ap()
        parts = [nc.dram_tensor(f"part{k}", [NP + P, F], F32).ap() for k in range(PARTS)]
        cnt_tab = nc.dram_tensor("cnt_tab", [J, P], F32).ap()

        def by_node(tab):
            return tab[0:NP, :].rearrange("(j p) f -> p j f", p=P)

        x_nm = sb(ctx, "x_nm", [P, J, F])
        h_nm = sb(ctx, "h_nm", [P, J, F])
        acc_t = sb(ctx, "acc_t", [P, NP])
        srcf = sb(ctx, "srcf", [P, TILES])
        dstf = sb(ctx, "dstf", [P, TILES + K])
        src_lo = sb(ctx, "src_lo", [P, TILES + K], BF16)
        src_hi = sb(ctx, "src_hi", [P, TILES + K], BF16)
        spare = sb(ctx, "spare", [P, TILES])
        dinv = sb(ctx, "dinv", [P, J])
        rcnt = sb(ctx, "rcnt", [P, J])
        base_all = sb(ctx, "base_all", [P, SUPERS + 1])
        meta = sb(ctx, "meta", [1, SUPERS], I32)
        meta_lag = sb(ctx, "meta_lag", [1, SUPERS], I32)
        cumx = sb(ctx, "cumx", [1, SUPERS], I32)
        ident = sb(ctx, "ident", [P, P])
        identb = sb(ctx, "identb", [P, P], BF16)
        iotab = sb(ctx, "iotab", [P, P], BF16)
        pidx = sb(ctx, "pidx", [P, 1])
        spare_row = sb(ctx, "spare_row", [P, 1])
        earlier = sb(ctx, "earlier", [P, P])
        zero_t = sb(ctx, "zero_t", [P, P])
        w0_sb = sb(ctx, "w0_sb", [P, P])
        w1ab_sb = sb(ctx, "w1ab_sb", [P, 2 * P])
        w1c_sb = sb(ctx, "w1c_sb", [EDGE_F + 1, F])
        w2_sb = sb(ctx, "w2_sb", [F + 1, F])
        wg_sb = sb(ctx, "wg_sb", [P, 4 * F])
        bg_sb = sb(ctx, "bg_sb", [P, 4 * F])
        w21_sb = sb(ctx, "w21_sb", [F, HID])
        b21_sb = sb(ctx, "b21_sb", [HID, 1])
        w22_sb = sb(ctx, "w22_sb", [HID, F])
        b22_sb = sb(ctx, "b22_sb", [P, F])
        eps1 = sb(ctx, "eps1", [P, 1])
        wl3_sb = sb(ctx, "wl3_sb", [F, F])
        wr3_sb = sb(ctx, "wr3_sb", [F + 1, F])

        passed = lasting_sem("passed")

        def hold(eng, semaphore, value):
            if not (isinstance(value, int) and value <= 0):
                eng.wait_ge(semaphore, value)
                eng.sem_inc(passed, 1)

        slot_done = [[lasting_sem(f"slot_done{b}_{k}") for k in range(K)] for b in range(2)]

        (centered, squared, var_ready, rooted, normed, table_stored, ln_small) = (
            lasting_sem(n) for n in ("centered", "squared", "var_ready", "rooted", "normed", "table_stored", "ln_small"))

        class Norm:

            def __init__(self, c, turn, scale=None, smalls_before=0):
                self.sq = sb(c, f"sq_{turn}", [P, J, F])
                self.st = sb(c, f"st_{turn}", [P, 5, J])
                self.scale = scale
                self.chunks_before = turn * CHUNKS
                self.smalls_before = smalls_before

            def vector(self, dve):
                st, before, n = self.st, self.chunks_before, self.smalls_before
                parts_of = [slice(c * JC, (c + 1) * JC) for c in range(CHUNKS)]
                for c, cc in enumerate(parts_of):
                    dve.tensor_reduce(st[:, 0, cc], x_nm[:, cc, :], AX_X, ALU.add).then_inc(ln_small, 1)
                    n += 1
                    dve.wait_ge(ln_small, n)
                    dve.tensor_scalar(st[:, 1, cc], st[:, 0, cc], -1.0 / F, None, ALU.mult).then_inc(ln_small, 1)
                    n += 1
                    dve.wait_ge(ln_small, n)
                    dve.tensor_tensor(h_nm[:, cc, :], x_nm[:, cc, :], st[:, 1, cc, None].to_broadcast([P, JC, F]),
                                      ALU.add).then_inc(centered, 1)
                for c, cc in enumerate(parts_of):
                    dve.wait_ge(squared, before + c + 1)
                    dve.tensor_reduce(st[:, 2, cc], self.sq[:, cc, :], AX_X, ALU.add).then_inc(ln_small, 1)
                    n += 1
                    dve.wait_ge(ln_small, n)
                    dve.tensor_scalar(st[:, 3, cc], st[:, 2, cc], 1.0 / F, EPS, ALU.mult,
                                      ALU.add).then_inc(var_ready, 1)
                for c, cc in enumerate(parts_of):
                    dve.wait_ge(rooted, before + c + 1)
                    dve.reciprocal(st[:, 1, cc], st[:, 4, cc]).then_inc(ln_small, 1)
                    n += 1
                    dve.wait_ge(ln_small, n)
                    if self.scale is not None:
                        dve.tensor_tensor(st[:, 1, cc], st[:, 1, cc], self.scale[:, cc], ALU.mult).then_inc(ln_small, 1)
                        n += 1
                        dve.wait_ge(ln_small, n)
                    dve.scalar_tensor_tensor(out=h_nm[:, cc, :], in0=h_nm[:, cc, :], scalar=0.0,
                                             in1=st[:, 1, cc, None].to_broadcast([P, JC, F]), op0=ALU.max,
                                             op1=ALU.mult).then_inc(normed, 1)

            def activation(self, act):
                before = self.chunks_before
                for c in range(CHUNKS):
                    cc = slice(c * JC, (c + 1) * JC)
                    act.wait_ge(centered, before + c + 1)
                    nc.scalar.activation(self.sq[:, cc, :], h_nm[:, cc, :], ACT.Square).then_inc(squared, 1)
                for c in range(CHUNKS):
                    cc = slice(c * JC, (c + 1) * JC)
                    act.wait_ge(var_ready, before + c + 1)
                    nc.scalar.activation(self.st[:, 4, cc], self.st[:, 3, cc], ACT.Sqrt).then_inc(rooted, 1)

            def store(self, sp, table, stored_before):
                for c in range(CHUNKS):
                    cc = slice(c * JC, (c + 1) * JC)
                    sp.wait_ge(normed, self.chunks_before + c + 1)
                    sp.dma_start(by_node(table)[:, cc, :], h_nm[:, cc, :]).then_inc(table_stored, 16)
                sp.wait_ge(table_stored, 16 * CHUNKS * (stored_before + 1))

        with ExitStack() as ph:
            norm = Norm(ph, 0, dinv)
            cols_i = sb(ph, "cols_i", [P, 2, TILES], I32)
            hi_b = sb(ph, "hi_b", [P, TILES], BF16)
            one_lo = sb(ph, "one_lo", [P, 2, P, K], BF16)
            one_hi = sb(ph, "one_hi", [P, 2, J, K], BF16)
            iota_k = sb(ph, "iota_k", [P, P, K], BF16)
            iota_i = sb(ph, "iota_i", [P, P], I32)
            pidx_i = sb(ph, "pidx_i", [P, 1], I32)
            zero_b = sb(ph, "zero_b", [P, J], BF16)
            bias_i = sb(ph, "bias_i", [P, 3 * F])
            range_p = sb(ph, "range_p", [P, 2, SUPERS])
            range_c = sb(ph, "range_c", [HALF, 2, 4])
            more_i = sb(ph, "more_i", [HALF, 2, 2], I32)
            rows = sb(ph, "rows", [1, 5, SUPERS])
            deg = sb(ph, "deg", [P, 3, J])
            ps_deg = psum(ph, "ps_deg", [P, 512])
            ps_t = psum(ph, "ps_t", [P, 4, P])
            ps_b = psum(ph, "ps_b", [P, 3, 2 * P])

            ids_in, x_loaded, w_loaded, biases_in = sem("ids_in"), sem("x_loaded"), sem("w_loaded"), sem("biases_in")
            iotas, zeros_ready, zeroed, idents = sem("iotas"), sem("zeros_ready"), sem("zeroed"), sem("idents")
            prep = sem("prep")
            ranges_ready, ranges_turned, range_cols, ranges_spread = (
                sem("ranges_ready"), sem("ranges_turned"), sem("range_cols"), sem("ranges_spread"))
            los, his, counted = sem("los"), sem("his"), sem("counted")
            zero_ready, codes_ready, deg_ready, deg_rooted = (
                sem("zero_ready"), sem("codes_ready"), sem("deg_ready"), sem("deg_rooted"))
            with nc.Block() as block:
                @block.sync
                def _(sp):
                    sp.dma_start(cols_i[:, 0, :], src_cols).then_inc(ids_in, 16)
                    sp.dma_start(cols_i[:, 1, :], dst_cols).then_inc(ids_in, 16)
                    sp.dma_start(x_nm[:, :, :], by_node(x_in)).then_inc(x_loaded, 16)
                    sp.wait_ge(zeros_ready, 1)
                    for k in range(PARTS):
                        sp.dma_start(parts[k].rearrange("(p j) f -> p (j f)", p=P),
                                     acc_t[:, 0:(J + 1) * F]).then_inc(zeroed, 16)
                    norm.store(sp, u_tab, 0)
                    sp.wait_ge(zeroed, 16 * PARTS)

                @block.gpsimd
                def _(pool):
                    pool.iota(iota_i[:, :], [[1, P]], base=0, channel_multiplier=0).then_inc(iotas, 1)
                    pool.iota(pidx_i[:, :], [[1, 1]], base=0, channel_multiplier=1).then_inc(iotas, 1)
                    pool.memset(zero_b[:, :], 0.0).then_inc(zero_ready, 1)
                    pool.memset(zero_t[:, :], 0.0).then_inc(zero_ready, 1)
                    pool.memset(acc_t[:, 0:(J + 1) * F], 0.0).then_inc(zeros_ready, 1)

                @block.scalar
                def _(act):
                    loads = ((w0_sb, w0bd), (w1ab_sb, w1ab), (w1c_sb, w1c), (w2_sb, w2b), (wg_sb, wgate),
                             (w21_sb, w21), (b21_sb, b21), (w22_sb, w22), (wl3_sb, wl3), (wr3_sb, wr3b))
                    for tile, source in loads:
                        act.dma_start(tile[:, :], source).then_inc(w_loaded, 16)
                    act.dma_start(b22_sb[:, :], b22.to_broadcast([P, F])).then_inc(w_loaded, 16)
                    act.dma_start(bias_i[:, :], bih.to_broadcast([P, 3 * F])).then_inc(biases_in, 16)
                    act.dma_start(bg_sb[:, 0:2 * F], bhh[:, 0:2 * F].to_broadcast([P, 2 * F])).then_inc(biases_in, 16)
                    act.dma_start(bg_sb[:, 3 * F:4 * F], bhh[:, 2 * F:3 * F].to_broadcast([P, F])).then_inc(biases_in, 16)
                    act.dma_start(eps1[:, :], eps_in.to_broadcast([P, 1])).then_inc(biases_in, 16)
                    act.wait_ge(w_loaded, 16 * (len(loads) + 1))
                    act.wait_ge(deg_ready, 1)
                    nc.scalar.activation(deg[:, 2, :], deg[:, 0, :], ACT.Sqrt).then_inc(deg_rooted, 1)
                    norm.activation(act)

                @block.vector
                def _(dve):
                    n = 0

                    def step(ins):
                        nonlocal n
                        n += 1
                        ins.then_inc(prep, 1)

                    def settled():
                        dve.wait_ge(prep, n)

                    dve.wait_ge(iotas, 2)
                    step(dve.tensor_copy(iotab[:, :], iota_i[:, :]))
                    step(dve.tensor_copy(pidx[:, :], pidx_i[:, :]))
                    settled()
                    step(dve.tensor_copy(iota_k[:, :, :], iotab[:, :, None].to_broadcast([P, P, K])))
                    step(dve.tensor_scalar(ident[:, :], iotab[:, :], pidx[:, 0:1], None, ALU.is_equal))
                    step(dve.tensor_scalar(identb[:, :], iotab[:, :], pidx[:, 0:1], None, ALU.is_equal))
                    step(dve.tensor_scalar(earlier[:, :], iotab[:, :], pidx[:, 0:1], None, ALU.is_lt))
                    step(dve.tensor_scalar(spare_row[:, :], pidx[:, :], float(NP), None, ALU.add))
                    settled()
                    dve.sem_inc(idents, 1)
                    dve.wait_ge(biases_in, 64)
                    step(dve.tensor_tensor(bg_sb[:, 0:2 * F], bg_sb[:, 0:2 * F], bias_i[:, 0:2 * F], ALU.add))
                    step(dve.tensor_copy(bg_sb[:, 2 * F:3 * F], bias_i[:, 2 * F:3 * F]))
                    step(dve.tensor_scalar(eps1[:, :], eps1[:, :], 1.0, None, ALU.add))
                    dve.wait_ge(ids_in, 32)
                    step(dve.tensor_copy(srcf[:, :], cols_i[:, 0, :]))
                    step(dve.tensor_copy(dstf[:, 0:TILES], cols_i[:, 1, :]))
                    settled()
                    step(dve.tensor_scalar(cols_i[:, 1, :], cols_i[:, 0, :], P - 1, None, ALU.bitwise_and))
                    step(dve.tensor_scalar(cols_i[:, 0, :], cols_i[:, 0, :], 7, None, ALU.arith_shift_right))
                    settled()
                    step(dve.tensor_copy(src_lo[:, 0:TILES], cols_i[:, 1, :]))
                    step(dve.tensor_copy(hi_b[:, :], cols_i[:, 0, :]))
                    step(dve.tensor_scalar(src_hi[:, 0:TILES], cols_i[:, 0, :], float(P), None, ALU.mult))
                    for ahead in (src_lo, src_hi, dstf):
                        step(dve.memset(ahead[:, TILES:TILES + K], 0.0))
                    step(dve.memset(base_all[:, SUPERS:SUPERS + 1], 0.0))
                    step(dve.tensor_scalar(spare[:, :], srcf[:, :], -1.0, spare_row[:, 0:1], ALU.mult, ALU.add))
                    by_step = dstf[:, 0:TILES].rearrange("p (s k) -> p s k", k=K)
                    dve.tensor_reduce(range_p[:, 0, :], by_step, AX_X, ALU.min).then_inc(ranges_ready, 1)
                    dve.tensor_reduce(range_p[:, 1, :], by_step, AX_X, ALU.max).then_inc(ranges_ready, 1)
                    settled()
                    dve.sem_inc(codes_ready, 1)

                    for i in first_then_loop(dve, HALF):
                        for b in range(2):
                            s = 2 * i + b
                            hold(dve, counted, s - 1)
                            dve.tensor_tensor(one_lo[:, b, :, :], iota_k[:, :, :],
                                              src_lo[:, None, bass.ds(s * K, K)].to_broadcast([P, P, K]),
                                              ALU.is_equal).then_inc(los, 1)
                            dve.tensor_tensor(one_hi[:, b, :, :], iota_k[:, 0:J, :],
                                              hi_b[:, None, bass.ds(s * K, K)].to_broadcast([P, J, K]),
                                              ALU.is_equal).then_inc(his, 1)

                    dve.wait_ge(ranges_turned, 1)
                    for c in range(2):
                        step(dve.tensor_reduce(range_c[:, c, 0:1], ps_t[0:HALF, c, :], AX_X, ALU.min))
                        step(dve.tensor_reduce(range_c[:, c, 1:2], ps_t[0:HALF, 2 + c, :], AX_X, ALU.max))
                    settled()
                    step(dve.tensor_tensor(range_c[:, :, 2], range_c[:, :, 1], range_c[:, :, 0], ALU.subtract))
                    settled()
                    step(dve.tensor_copy(more_i[:, 0, :], range_c[:, :, 2]))
                    settled()
                    step(dve.tensor_scalar(more_i[:, 1, :], more_i[:, 0, :], 7, None, ALU.arith_shift_right))
                    settled()
                    step(dve.tensor_copy(range_c[:, :, 2], more_i[:, 1, :]))
                    settled()
                    step(dve.scalar_tensor_tensor(out=range_c[:, :, 3], in0=range_c[:, :, 0], scalar=float(PACK),
                                                  in1=range_c[:, :, 2], op0=ALU.mult, op1=ALU.add))
                    settled()
                    dve.sem_inc(range_cols, 1)
                    dve.wait_ge(ranges_spread, 1)
                    for c in range(2):
                        half = slice(c * HALF, (c + 1) * HALF)
                        step(dve.tensor_copy(base_all[:, half], ps_b[:, 0, c * P:c * P + HALF]))
                        step(dve.tensor_copy(rows[:, 0, half], ps_b[0:1, 1, c * P:c * P + HALF]))
                        step(dve.tensor_copy(meta[:, half], ps_b[0:1, 2, c * P:c * P + HALF]))
                    settled()
                    step(dve.tensor_tensor_scan(rows[:, 1, :], rows[:, 0, :], rows[:, 0, :], 0.0, ALU.add, ALU.bypass))
                    settled()
                    step(dve.tensor_tensor(rows[:, 2, :], rows[:, 1, :], rows[:, 0, :], ALU.subtract))
                    settled()
                    step(dve.tensor_copy(cumx[:, :], rows[:, 2, :]))
                    step(dve.tensor_tensor(rows[:, 3, 1:SUPERS], rows[:, 0, 1:SUPERS], rows[:, 0, 0:SUPERS - 1], ALU.add))
                    settled()
                    step(dve.tensor_scalar(rows[:, 4, 1:SUPERS], rows[:, 3, 1:SUPERS], float(PACK - 1), None, ALU.min))
                    settled()
                    step(dve.scalar_tensor_tensor(out=meta_lag[:, 1:SUPERS], in0=base_all[0:1, 0:SUPERS - 1],
                                                  scalar=float(PACK), in1=rows[:, 4, 1:SUPERS], op0=ALU.mult, op1=ALU.add))
                    step(dve.tensor_copy(meta_lag[:, 0:1], rows[:, 0, 0:1]))

                    dve.wait_ge(counted, SUPERS)
                    step(dve.tensor_scalar(deg[:, 0, :], ps_deg[:, 0:J], 1.0, None, ALU.max))
                    step(dve.tensor_scalar(deg[:, 1, :], ps_deg[:, 0:J], 0.0, None, ALU.is_gt))
                    settled()
                    dve.sem_inc(deg_ready, 1)
                    dve.wait_ge(deg_rooted, 1)
                    step(dve.reciprocal(dinv[:, :], deg[:, 2, :]))
                    settled()
                    step(dve.tensor_tensor(dinv[:, :], dinv[:, :], deg[:, 1, :], ALU.mult))
                    settled()
                    dve.wait_ge(x_loaded, 16)
                    norm.vector(dve)

                @block.tensor
                def _(pe):
                    pe.wait_ge(idents, 1)
                    pe.wait_ge(zero_ready, 1)
                    pe.wait_ge(ranges_ready, 2)
                    for c in range(2):
                        for m in range(2):
                            last = pe.transpose(ps_t[0:HALF, 2 * m + c, :], range_p[:, m, c * HALF:(c + 1) * HALF],
                                                ident[:, :])
                    last.then_inc(ranges_turned, 1)
                    pe.matmul(ps_deg[:, 0:J], identb[:, :], zero_b[:, 0:J], start=True, stop=False,
                              skip_group_check=True)
                    for i in first_then_loop(pe, HALF):
                        for b in range(2):
                            s = 2 * i + b
                            pe.wait_ge(los, s + 1)
                            pe.wait_ge(his, s + 1)
                            for k in range(K):
                                last = pe.matmul(ps_deg[:, 0:J], one_lo[:, b, :, k], one_hi[:, b, :, k], start=False,
                                                 stop=False, skip_group_check=True)
                            last.then_inc(counted, 1)
                    pe.wait_ge(range_cols, 1)
                    for c in range(2):
                        for row, column in enumerate((0, 2, 3)):
                            last = pe.matmul(ps_b[:, row, c * P:c * P + HALF],
                                             range_c[:, c, column:column + 1].to_broadcast([HALF, P]),
                                             ident[0:HALF, 0:HALF], start=True, stop=True)
                    last.then_inc(ranges_spread, 1)

        def window_parts_of(s, eng, table=meta):
            word = eng.value_load(table[0:1, bass.ds(s, 1)], min_val=0, max_val=BASE_MAX * PACK + PACK - 1)
            return word // PACK, word % PACK

        def window_parts(i, b, eng, table=meta):
            return window_parts_of(2 * i + b, eng, table)

        def before(eng, s):
            return eng.value_load(cumx[0:1, bass.ds(s, 1)], min_val=0, max_val=SUPERS * P)

        def further(eng, base, w):
            return nc.s_assert_within(base + (w + 1) * P, 0, BASE_MAX, skip_runtime_bounds_check_because=
                                      "windows end with the one that holds the greatest destination")
        end_stage()

        with ExitStack() as ph:
            rel = sb(ph, "rel", [P, 2, K])
            relb = sb(ph, "relb", [P, 2, K], BF16)
            relx = sb(ph, "relx", [P, K])
            relxb = sb(ph, "relxb", [P, K], BF16)
            hot_t = sb(ph, "hot_t", [P, 2, K, P])
            same = sb(ph, "same", [P, 2, K, P])
            dup = sb(ph, "dup", [P, K, P])
            ndup = sb(ph, "ndup", [P, 2, K])
            row_at = sb(ph, "row_at", [P, 2, K], I32)
            u_win = sb(ph, "u_win", [P, 2, F])
            msg = sb(ph, "msg", [P, 2, K, F])
            total = sb(ph, "total", [P, 2, K, F])
            ps_dst = psum(ph, "ps_dst", [P, K, P])
            ps_src = psum(ph, "ps_src", [P, K, P])
            ps_msg = psum(ph, "ps_msg", [P, 2, K, F])
            ps_tot = psum(ph, "ps_tot", [P, 2, K, F])

            win_in = [sem(f"l0_win_in{b}") for b in range(2)]
            win_x, rel_f, rel_ready, dst_spread, src_spread = (
                sem(f"l0_{n}") for n in ("win_x", "rel_f", "rel_ready", "dst_spread", "src_spread"))
            hot_ready, same_ready, dup_ready, ndup_ready, small, at_ready = (
                sem(f"l0_{n}") for n in ("hot_ready", "same_ready", "dup_ready", "ndup_ready", "small", "at_ready"))
            relx_ready, dstx_spread, hotx_ready, msgx_done = (
                sem(f"l0_{n}") for n in ("relx_ready", "dstx_spread", "hotx_ready", "msgx_done"))
            msg_main, msg_done, msg_copied, tot_done, tot_copied = (
                sem(f"l0_{n}") for n in ("msg_main", "msg_done", "msg_copied", "tot_done", "tot_copied"))
            with nc.Block() as block:
                @block.sync
                def _(sp):
                    for i in first_then_loop(sp, HALF):
                        for b in range(2):
                            s = 2 * i + b
                            base, more = window_parts(i, b, sp)
                            hold(sp, msg_done, s - 1)
                            sp.dma_start(u_win[:, b, :], u_tab[bass.ds(base, P), :]).then_inc(win_in[b], 16)
                            with sp.If(more > 0):
                                seen = before(sp, s)
                                with sp.Fori(0, more) as w:
                                    hold(sp, msg_main, s + 1)
                                    hold(sp, msgx_done, seen + w + 1)
                                    sp.dma_start(u_win[:, b, :],
                                                 u_tab[bass.ds(further(sp, base, w), P), :]).then_inc(win_x, 16)
                                    hold(sp, win_x, (seen + w + 1) * 16)

                @block.vector
                def _(dve):
                    def relate(b, s):
                        need(dve, dst_spread, s - 1)
                        dve.tensor_scalar(rel[:, b, :], dstf[:, bass.ds(s * K, K)], base_all[:, bass.ds(s, 1)], -1.0,
                                          ALU.subtract, ALU.max).then_inc(rel_f, 1)
                        dve.wait_ge(rel_f, s + 1)
                        dve.tensor_scalar(relb[:, b, :], rel[:, b, :], float(P), None, ALU.min).then_inc(rel_ready, 1)

                    relate(0, 0)
                    for i in first_then_loop(dve, HALF):
                        for b in range(2):
                            s = 2 * i + b
                            tiles = bass.ds(s * K, K)
                            word = dve.value_load(meta[0:1, bass.ds(s, 1)], min_val=0, max_val=BASE_MAX * PACK + PACK - 1)
                            more = word % PACK
                            need(dve, msg_done, s - 1)
                            dve.wait_ge(dst_spread, s + 1)
                            dve.tensor_scalar(hot_t[:, b, :, :], ps_dst[:, :, :], pidx[:, 0:1], None,
                                              ALU.is_equal).then_inc(hot_ready, 1)
                            need(dve, tot_done, s - 1)
                            dve.wait_ge(src_spread, s + 1)
                            dve.tensor_tensor(same[:, b, :, :], ps_src[:, :, :],
                                              srcf[:, tiles, None].to_broadcast([P, K, P]),
                                              ALU.is_equal).then_inc(same_ready, 1)
                            need(dve, ndup_ready, s)
                            dve.wait_ge(same_ready, s + 1)
                            dve.tensor_tensor(dup[:, :, :], same[:, b, :, :],
                                              earlier[:, None, :].to_broadcast([P, K, P]), ALU.mult).then_inc(dup_ready, 1)
                            need(dve, small, s)
                            dve.wait_ge(dup_ready, s + 1)
                            dve.tensor_reduce(ndup[:, 0, :], dup[:, :, :], AX_X, ALU.add).then_inc(ndup_ready, 1)
                            need(dve, at_ready, s)
                            dve.wait_ge(ndup_ready, s + 1)
                            dve.scalar_tensor_tensor(out=ndup[:, 1, :], in0=ndup[:, 0, :], scalar=0.0,
                                                     in1=spare[:, tiles], op0=ALU.is_gt, op1=ALU.mult).then_inc(small, 1)
                            for k in range(PARTS, K):
                                need(dve, slot_done[b][k], 16 * i)
                            dve.wait_ge(small, s + 1)
                            dve.tensor_tensor(row_at[:, b, :], ndup[:, 1, :], srcf[:, tiles], ALU.add).then_inc(at_ready, 1)
                            with dve.If(more > 0):
                                seen = before(dve, s)
                                dve.tensor_copy(relx[:, :], rel[:, b, :])
                                dve.drain()
                                with dve.Fori(0, more) as w:
                                    hold(dve, dstx_spread, seen + w + 1)
                                    dve.tensor_scalar(relx[:, :], relx[:, :], -float(P), None, ALU.add)
                                    dve.drain()
                                    dve.tensor_scalar(relxb[:, :], relx[:, :], -1.0, float(P), ALU.max,
                                                      ALU.min).then_inc(relx_ready, 1)
                                    hold(dve, msg_main, s + 1)
                                    hold(dve, msgx_done, seen + w + 1)
                                    hold(dve, dstx_spread, seen + w + 2)
                                    dve.tensor_scalar(hot_t[:, b, :, :], ps_dst[:, :, :], pidx[:, 0:1], None,
                                                      ALU.is_equal).then_inc(hotx_ready, 1)
                                    dve.drain()
                            relate(1 - b, s + 1)

                @block.tensor
                def _(pe):
                    def spread(b, s):
                        need(pe, hot_ready, s)
                        pe.wait_ge(rel_ready, s + 1)
                        for k in range(K):
                            last = pe.matmul(ps_dst[:, k, :], relb[:, b, k:k + 1].to_broadcast([P, P]), identb[:, :],
                                             start=True, stop=True)
                        last.then_inc(dst_spread, 1)
                        hold(pe, same_ready, s)
                        for k in range(K):
                            for half, of_node in enumerate((src_lo, src_hi)):
                                last = pe.matmul(ps_src[:, k, :], of_node[:, bass.ds(s * K + k, 1)].to_broadcast([P, P]),
                                                 identb[:, :], start=(half == 0), stop=(half == 1))
                        last.then_inc(src_spread, 1)

                    def sum_tile_sources(b, s):
                        need(pe, tot_copied, s - 1)
                        pe.wait_ge(same_ready, s + 1)
                        pe.wait_ge(msg_copied, s + 1)
                        for k in range(K):
                            last = pe.matmul(ps_tot[:, b, k, :], same[:, b, k, :], msg[:, b, k, :], start=True, stop=True)
                        last.then_inc(tot_done, 1)

                    pe.sem_inc(dstx_spread, 1)
                    pe.sem_inc(msgx_done, 1)
                    spread(0, 0)
                    for i in first_then_loop(pe, HALF):
                        for b in range(2):
                            s = 2 * i + b
                            word = pe.value_load(meta[0:1, bass.ds(s, 1)], min_val=0, max_val=BASE_MAX * PACK + PACK - 1)
                            more = word % PACK
                            if not (isinstance(s, int) and s == 0):
                                sum_tile_sources(1 - b, s - 1)
                            need(pe, msg_copied, s - 1)
                            pe.wait_ge(win_in[b], 16 * i + 16)
                            pe.wait_ge(hot_ready, s + 1)
                            for k in range(K):
                                last = pe.matmul(ps_msg[:, b, k, :], hot_t[:, b, k, :], u_win[:, b, :], start=(k == 0),
                                                 stop=False, skip_group_check=True)
                            last.then_inc(msg_main, 1)
                            with pe.If(more > 0):
                                seen = before(pe, s)
                                with pe.Fori(0, more) as w:
                                    hold(pe, relx_ready, seen + w + 1)
                                    for k in range(K):
                                        last = pe.matmul(ps_dst[:, k, :], relxb[:, k:k + 1].to_broadcast([P, P]),
                                                         identb[:, :], start=True, stop=True)
                                    last.then_inc(dstx_spread, 1)
                                    hold(pe, hotx_ready, seen + w + 1)
                                    hold(pe, win_x, (seen + w + 1) * 16)
                                    for k in range(K):
                                        last = pe.matmul(ps_msg[:, b, k, :], hot_t[:, b, k, :], u_win[:, b, :],
                                                         start=False, stop=False, skip_group_check=True)
                                    last.then_inc(msgx_done, 1)
                            pe.matmul(ps_msg[:, b, K - 1, :], zero_t[:, :], u_win[:, b, :], start=False, stop=True,
                                      skip_group_check=True).then_inc(msg_done, 1)
                            spread(1 - b, s + 1)
                    sum_tile_sources(1, SUPERS - 1)

                @block.scalar
                def _(act):
                    def copy_total(b, s, i_of):
                        act.wait_ge(tot_done, s + 1)
                        for k in range(PARTS, K):
                            hold(act, slot_done[b][k], 16 * i_of)
                        nc.scalar.activation(total[:, b, :, :], ps_tot[:, b, :, :], ACT.Copy).then_inc(tot_copied, 1)

                    for i in first_then_loop(act, HALF):
                        for b in range(2):
                            s = 2 * i + b
                            if not (isinstance(s, int) and s == 0):
                                copy_total(1 - b, s - 1, i if b else i - 1)
                            hold(act, msg_done, s + 1)
                            hold(act, tot_done, s - 1)
                            nc.scalar.activation(msg[:, b, :, :], ps_msg[:, b, :, :], ACT.Copy).then_inc(msg_copied, 1)
                    copy_total(1, SUPERS - 1, HALF - 1)

                @block.gpsimd
                def _(pool):
                    for i in first_then_loop(pool, HALF):
                        for b in range(2):
                            s = 2 * i + b
                            hold(pool, at_ready, s + 1)
                            hold(pool, tot_copied, s + 1)
                            for k in range(K):
                                if k >= PARTS:
                                    hold(pool, slot_done[b][k - PARTS], 16 * i + 16)
                                else:
                                    hold(pool, slot_done[1 - b][k + PARTS], 16 * i + (16 if b else 0))
                                pool.indirect_dma_start(
                                    parts[k % PARTS][:, :], bass.IndirectOffsetOnAxis(ap=row_at[:, b, k:k + 1], axis=0),
                                    total[:, b, k, :], None, compute_op=ALU.add).then_inc(slot_done[b][k], 16)
                    for b in range(2):
                        for k in range(K):
                            pool.wait_ge(slot_done[b][k], 16 * HALF)
        end_stage()

        with ExitStack() as ph:
            sums = [acc_t[:, 0:J * F].rearrange("p (j f) -> p j f", f=F),
                    acc_t[:, J * F:2 * J * F].rearrange("p (j f) -> p j f", f=F)]
            c3 = ExitStack()
            sums += [sb(c3, f"sum{k}", [P, J, F])[:, :, :] for k in (2, 3)]
            agg = sb(c3, "agg", [P, 2, JG, F])
            agg_t = sb(c3, "agg_t", [P, 2, 2, P])
            upd = sb(c3, "upd", [P, 2, JG, F])
            ps_at = psum(c3, "ps_at", [P, 2, 4, P])
            ps_out = psum(c3, "ps_out", [P, 2, 8, F])
            HJ = J // 2
            parts_in, pairs_added, agg_ready, agg_turned, agg_t_ready, out_ready, upd_ready, x_updated = (
                sem(f"n0_{n}") for n in ("parts_in", "pairs_added", "agg_ready", "agg_turned", "agg_t_ready",
                                         "out_ready", "upd_ready", "x_updated"))
            part_in = [[sem(f"n0_part{k}_{c}") for c in range(2)] for k in range(PARTS)]
            with nc.Block() as block:
                @block.sync
                def _(sp):
                    for c in range(2):
                        for k in range(PARTS):
                            sp.dma_start(sums[k][:, c * HJ:(c + 1) * HJ, :],
                                         by_node(parts[k])[:, c * HJ:(c + 1) * HJ, :]).then_inc(part_in[k][c], 16)

                @block.gpsimd
                def _(pool):
                    for c in range(2):
                        for k in (2, 3):
                            pool.wait_ge(part_in[k][c], 16)
                        cc = slice(c * HJ, (c + 1) * HJ)
                        pool.tensor_tensor(sums[2][:, cc, :], sums[2][:, cc, :], sums[3][:, cc, :],
                                           ALU.add).then_inc(pairs_added, 1)

                @block.vector
                def _(dve):
                    for c in range(2):
                        for k in (0, 1):
                            dve.wait_ge(part_in[k][c], 16)
                        cc = slice(c * HJ, (c + 1) * HJ)
                        dve.tensor_tensor(sums[0][:, cc, :], sums[0][:, cc, :], sums[1][:, cc, :],
                                          ALU.add).then_inc(pairs_added, 1)
                    dve.wait_ge(pairs_added, 4)

                    def update(b, g):
                        dve.wait_ge(out_ready, g + 1)
                        dve.tensor_tensor(upd[:, b, :, :], ps_out[:, b, 0:JG, :],
                                          dinv[:, bass.ds(g * JG, JG), None].to_broadcast([P, JG, F]),
                                          ALU.mult).then_inc(upd_ready, 1)
                        dve.wait_ge(upd_ready, g + 1)
                        cols = bass.ds(g * JG, JG)
                        dve.tensor_tensor(x_nm[:, cols, :], x_nm[:, cols, :], upd[:, b, :, :],
                                          ALU.add).then_inc(x_updated, 1)

                    for i in first_then_loop(dve, GROUPS // 2):
                        for b in range(2):
                            g = 2 * i + b
                            cols = bass.ds(g * JG, JG)
                            need(dve, agg_turned, g - 1)
                            dve.tensor_tensor(agg[:, b, :, :], sums[0][:, cols, :], sums[2][:, cols, :],
                                              ALU.add).then_inc(agg_ready, 1)
                            if not (isinstance(g, int) and g == 0):
                                update(1 - b, g - 1)
                    update(1, GROUPS - 1)
                    dve.wait_ge(x_updated, GROUPS)

                @block.tensor
                def _(pe):
                    for i in first_then_loop(pe, GROUPS // 2):
                        for b in range(2):
                            g = 2 * i + b
                            pe.wait_ge(agg_ready, g + 1)
                            need(pe, agg_t_ready, g - 1)
                            for q in range(2):
                                last = pe.transpose(ps_at[:, b, q, :],
                                                    agg[:, b, 2 * q:2 * q + 2, :].rearrange("p a f -> p (a f)"),
                                                    ident[:, :])
                            last.then_inc(agg_turned, 1)
                            pe.wait_ge(agg_t_ready, g + 1)
                            need(pe, upd_ready, g - 1)
                            for q in range(2):
                                last = pe.matmul(ps_out[:, b, 2 * q:2 * q + 2, :].rearrange("p a f -> p (a f)"),
                                                 agg_t[:, b, q, :], w0_sb[:, :], start=True, stop=True)
                            last.then_inc(out_ready, 1)

                @block.scalar
                def _(act):
                    for i in first_then_loop(act, GROUPS // 2):
                        for b in range(2):
                            g = 2 * i + b
                            act.wait_ge(agg_turned, g + 1)
                            need(act, out_ready, g - 1)
                            nc.scalar.activation(agg_t[:, b, :, :], ps_at[:, b, 0:2, :], ACT.Copy).then_inc(agg_t_ready, 1)
            c3.close()

            norm = Norm(ph, 1, smalls_before=5 * CHUNKS)
            h_st = sb(ph, "h_st", [P, 2, JG, F])
            h_t = sb(ph, "h_t", [P, 2, 2, P])
            ab = sb(ph, "ab", [P, 2, 2, JG, F])
            ps_ht = psum(ph, "ps_ht", [P, 2, 4, P])
            ps_ab = psum(ph, "ps_ab", [P, 2, 2, 4 * F])
            staged, turned, turned_copied, ab_done, ab_copied = (
                sem(f"n1_{n}") for n in ("staged", "turned", "turned_copied", "ab_done", "ab_copied"))
            ab_out = [sem(f"n1_ab_out{b}") for b in range(2)]
            with nc.Block() as block:
                @block.vector
                def _(dve):
                    norm.vector(dve)
                    for i in first_then_loop(dve, GROUPS // 2):
                        for b in range(2):
                            g = 2 * i + b
                            dve.wait_ge(ab_done, g + 1)
                            need(dve, ab_out[b], 32 * i)
                            dve.tensor_copy(ab[:, b, :, :, :].rearrange("p e (q c) f -> p q e (c f)", c=2),
                                            ps_ab[:, b, :, :].rearrange("p q (e m) -> p q e m", e=2)
                                            ).then_inc(ab_copied, 1)

                @block.gpsimd
                def _(pool):
                    pool.wait_ge(normed, 2 * CHUNKS)
                    for i in first_then_loop(pool, GROUPS // 2):
                        for b in range(2):
                            g = 2 * i + b
                            hold(pool, turned, g - 1)
                            pool.tensor_copy(h_st[:, b, :, :], h_nm[:, bass.ds(g * JG, JG), :]).then_inc(staged, 1)

                @block.tensor
                def _(pe):
                    for i in first_then_loop(pe, GROUPS // 2):
                        for b in range(2):
                            g = 2 * i + b
                            pe.wait_ge(staged, g + 1)
                            need(pe, turned_copied, g - 1)
                            for q in range(2):
                                last = pe.transpose(ps_ht[:, b, q, :],
                                                    h_st[:, b, 2 * q:2 * q + 2, :].rearrange("p a f -> p (a f)"),
                                                    ident[:, :])
                            last.then_inc(turned, 1)
                            pe.wait_ge(turned_copied, g + 1)
                            need(pe, ab_copied, g - 1)
                            for q in range(2):
                                last = pe.matmul(ps_ab[:, b, q, :], h_t[:, b, q, :], w1ab_sb[:, :], start=True, stop=True)
                            last.then_inc(ab_done, 1)

                @block.scalar
                def _(act):
                    norm.activation(act)
                    for i in first_then_loop(act, GROUPS // 2):
                        for b in range(2):
                            g = 2 * i + b
                            act.wait_ge(turned, g + 1)
                            need(act, ab_done, g - 1)
                            nc.scalar.activation(h_t[:, b, :, :], ps_ht[:, b, 0:2, :], ACT.Copy).then_inc(turned_copied, 1)

                @block.sync
                def _(sp):
                    for i in first_then_loop(sp, GROUPS // 2):
                        for b in range(2):
                            g = 2 * i + b
                            hold(sp, ab_copied, g + 1)
                            for end, tab in enumerate((a_tab, b_tab)):
                                rows_of = tab[bass.ds(g * GN, GN), :].rearrange("(j p) f -> p j f", p=P)
                                sp.dma_start(rows_of, ab[:, b, end, :, :]).then_inc(ab_out[b], 16)
                    for b in range(2):
                        sp.wait_ge(ab_out[b], 32 * (GROUPS // 2))

        def gather_slots(pool, idx_in, idx, table, dest, used):
            for i in first_then_loop(pool, HALF):
                for b in range(2):
                    s = 2 * i + b
                    hold(pool, used, s - 1)
                    hold(pool, idx_in[b], 16 * i + 16)
                    for k in range(K):
                        pool.indirect_dma_start(
                            dest[:, b, k, :], None, table[:, :],
                            bass.IndirectOffsetOnAxis(ap=idx[:, b, k:k + 1], axis=0)).then_inc(slot_done[b][k], 16)
        end_stage()

        with ExitStack() as ph:
            idx = sb(ph, "idx1", [P, 2, K], I32)
            edge = sb(ph, "edge", [EDGE_F + 1, 2, ST])
            b_win = sb(ph, "b_win", [P, 2, F])
            a_rows = sb(ph, "a_rows", [P, 2, K, F])
            rel = sb(ph, "rel1", [P, 2, K])
            relb = sb(ph, "relb1", [P, 2, K], BF16)
            relx = sb(ph, "relx1", [P, K])
            relxb = sb(ph, "relxb1", [P, K], BF16)
            hot_t = sb(ph, "hot_t1", [P, 2, K, P])
            hot = sb(ph, "hot1", [P, 2, K, P])
            act_rows = sb(ph, "act_rows", [P, 2, K, F + 1])
            ps_dst = psum(ph, "ps_dst1", [P, K, P])
            ps_pre = psum(ph, "ps_pre", [P, 2, K, F])
            ps_seg = psum(ph, "ps_seg1", [P, 2, 4, P])
            idx_in, win_in, edge_in = ([sem(f"l1_{n}{b}") for b in range(2)] for n in ("idx_in", "win_in", "edge_in"))
            cleared, ones_ready, win_x, rel_f, rel_ready, dst_spread, hot_t_ready, hot_ready = (
                sem(f"l1_{n}") for n in ("cleared", "ones_ready", "win_x", "rel_f", "rel_ready", "dst_spread",
                                         "hot_t_ready", "hot_ready"))
            relx_ready, dstx_spread, hotx_ready, prex_done, segx_hot, segx_done = (
                sem(f"l1_{n}") for n in ("relx_ready", "dstx_spread", "hotx_ready", "prex_done", "segx_hot", "segx_done"))
            pre_main, pre_done, act_ready, seg_main, seg_done, acc_done = (
                sem(f"l1_{n}") for n in ("pre_main", "pre_done", "act_ready", "seg_main", "seg_done", "acc_done"))
            with nc.Block() as block:
                @block.sync
                def _(sp):
                    for i in first_then_loop(sp, HALF):
                        for b in range(2):
                            s = 2 * i + b
                            base, more = window_parts(i, b, sp)
                            hold(sp, slot_done[b][K - 1], ROUND + 16 * i)
                            sp.dma_start(idx[:, b, :], src_steps[bass.ds(s, 1), :, :].rearrange("s p k -> p (s k)")
                                         ).then_inc(idx_in[b], 16)
                            hold(sp, pre_done, s - 1)
                            sp.dma_start(edge[:, b, :], edge_t[:, bass.ds(s * ST, ST)]).then_inc(edge_in[b], 16)
                            sp.dma_start(b_win[:, b, :], b_tab[bass.ds(base, P), :]).then_inc(win_in[b], 16)
                            with sp.If(more > 0):
                                seen = before(sp, s)
                                with sp.Fori(0, more) as w:
                                    hold(sp, pre_main, s + 1)
                                    hold(sp, prex_done, seen + w + 1)
                                    sp.dma_start(b_win[:, b, :],
                                                 b_tab[bass.ds(further(sp, base, w), P), :]).then_inc(win_x, 16)
                                    hold(sp, win_x, (seen + w + 1) * 16)

                @block.gpsimd
                def _(pool):
                    gather_slots(pool, idx_in, idx, a_tab, a_rows, pre_done)

                @block.vector
                def _(dve):
                    dve.memset(acc_t[:, :], 0.0).then_inc(cleared, 1)
                    dve.memset(act_rows[:, :, :, :], 1.0).then_inc(ones_ready, 1)
                    dve.wait_ge(cleared, 1)

                    def relate(b, s):
                        need(dve, dst_spread, s - 1)
                        need(dve, hot_ready, s - 1)
                        dve.tensor_scalar(rel[:, b, :], dstf[:, bass.ds(s * K, K)], base_all[:, bass.ds(s, 1)], -1.0,
                                          ALU.subtract, ALU.max).then_inc(rel_f, 1)
                        dve.wait_ge(rel_f, s + 1)
                        dve.tensor_scalar(relb[:, b, :], rel[:, b, :], float(P), None, ALU.min).then_inc(rel_ready, 1)

                    def accumulate(b, s, base):
                        cols = acc_t[0:F + 1, bass.ds(base, P)]
                        need(dve, acc_done, s)
                        dve.wait_ge(seg_main, s + 1)
                        dve.tensor_tensor(cols, cols, ps_seg[0:F + 1, b, 0, :], ALU.add).then_inc(acc_done, 1)

                    def further_sums(b, s):
                        base, more = window_parts_of(s, dve)
                        with dve.If(more > 0):
                            seen = before(dve, s)
                            hold(dve, acc_done, s + 1)
                            dve.tensor_copy(relx[:, :], rel[:, b, :])
                            dve.drain()
                            with dve.Fori(0, more) as w:
                                hold(dve, segx_done, seen + w + 1)
                                dve.tensor_scalar(relx[:, :], relx[:, :], -float(P), None, ALU.add)
                                dve.drain()
                                dve.tensor_tensor(hot[:, b, :, :], iotab[:, None, :].to_broadcast([P, K, P]),
                                                  relx[:, :, None].to_broadcast([P, K, P]),
                                                  ALU.is_equal).then_inc(segx_hot, 1)
                                hold(dve, segx_done, seen + w + 2)
                                far = acc_t[0:F + 1, bass.ds(further(dve, base, w), P)]
                                dve.tensor_tensor(far, far, ps_seg[0:F + 1, b, 0, :], ALU.add)
                                dve.drain()

                    relate(0, 0)
                    for i in first_then_loop(dve, HALF):
                        for b in range(2):
                            s = 2 * i + b
                            last_base, more = window_parts(i, b, dve, meta_lag)
                            need(dve, pre_done, s - 1)
                            dve.wait_ge(dst_spread, s + 1)
                            dve.tensor_scalar(hot_t[:, b, :, :], ps_dst[:, :, :], pidx[:, 0:1], None,
                                              ALU.is_equal).then_inc(hot_t_ready, 1)
                            need(dve, seg_done, s - 1)
                            dve.wait_ge(rel_f, s + 1)
                            dve.tensor_tensor(hot[:, b, :, :], iotab[:, None, :].to_broadcast([P, K, P]),
                                              rel[:, b, :, None].to_broadcast([P, K, P]), ALU.is_equal).then_inc(hot_ready, 1)
                            if not (isinstance(s, int) and s == 0):
                                accumulate(1 - b, s - 1, last_base)
                            with dve.If(more > 0):
                                if not (isinstance(s, int) and s == 0):
                                    further_sums(1 - b, s - 1)
                                own_more = dve.value_load(meta[0:1, bass.ds(s, 1)], min_val=0,
                                                          max_val=BASE_MAX * PACK + PACK - 1) % PACK
                                with dve.If(own_more > 0):
                                    seen = before(dve, s)
                                    dve.tensor_copy(relx[:, :], rel[:, b, :])
                                    dve.drain()
                                    with dve.Fori(0, own_more) as w:
                                        hold(dve, dstx_spread, seen + w + 1)
                                        dve.tensor_scalar(relx[:, :], relx[:, :], -float(P), None, ALU.add)
                                        dve.drain()
                                        dve.tensor_scalar(relxb[:, :], relx[:, :], -1.0, float(P), ALU.max,
                                                          ALU.min).then_inc(relx_ready, 1)
                                        hold(dve, pre_main, s + 1)
                                        hold(dve, prex_done, seen + w + 1)
                                        hold(dve, dstx_spread, seen + w + 2)
                                        dve.tensor_scalar(hot_t[:, b, :, :], ps_dst[:, :, :], pidx[:, 0:1], None,
                                                          ALU.is_equal).then_inc(hotx_ready, 1)
                                        dve.drain()
                                dve.drain()
                            relate(1 - b, s + 1)
                    base, more = window_parts(HALF - 1, 1, dve)
                    accumulate(1, SUPERS - 1, base)
                    further_sums(1, SUPERS - 1)

                @block.tensor
                def _(pe):
                    def spread(b, s):
                        need(pe, hot_t_ready, s)
                        pe.wait_ge(rel_ready, s + 1)
                        for k in range(K):
                            last = pe.matmul(ps_dst[:, k, :], relb[:, b, k:k + 1].to_broadcast([P, P]), identb[:, :],
                                             start=True, stop=True)
                        last.then_inc(dst_spread, 1)

                    def sum_by_node(b, s):
                        need(pe, acc_done, s - 1)
                        pe.wait_ge(hot_ready, s + 1)
                        pe.wait_ge(act_ready, s + 1)
                        for k in range(K):
                            last = pe.matmul(ps_seg[0:F + 1, b, 0, :], act_rows[:, b, k, :], hot[:, b, k, :],
                                             start=(k == 0), stop=(k == K - 1))
                        last.then_inc(seg_main, 1)

                    def further_sums(b, s):
                        base, more = window_parts_of(s, pe)
                        with pe.If(more > 0):
                            seen = before(pe, s)
                            with pe.Fori(0, more) as w:
                                hold(pe, segx_hot, seen + w + 1)
                                for k in range(K):
                                    last = pe.matmul(ps_seg[0:F + 1, b, 0, :], act_rows[:, b, k, :], hot[:, b, k, :],
                                                     start=(k == 0), stop=(k == K - 1))
                                last.then_inc(segx_done, 1)

                    for started in (dstx_spread, prex_done, segx_done):
                        pe.sem_inc(started, 1)
                    spread(0, 0)
                    for i in first_then_loop(pe, HALF):
                        for b in range(2):
                            s = 2 * i + b
                            last_base, more = window_parts(i, b, pe, meta_lag)
                            first = isinstance(s, int) and s == 0
                            if not first:
                                sum_by_node(1 - b, s - 1)
                            hold(pe, act_ready, s - 1)
                            hold(pe, edge_in[b], 16 * i + 16)
                            for k in range(K):
                                pe.matmul(ps_pre[:, b, k, :], edge[:, b, k * P:(k + 1) * P], w1c_sb[:, :],
                                          start=(k == 0), stop=False, skip_group_check=True)
                            pe.wait_ge(win_in[b], 16 * i + 16)
                            pe.wait_ge(hot_t_ready, s + 1)
                            for k in range(K):
                                last = pe.matmul(ps_pre[:, b, k, :], hot_t[:, b, k, :], b_win[:, b, :], start=False,
                                                 stop=False, skip_group_check=True)
                            last.then_inc(pre_main, 1)
                            with pe.If(more > 0):
                                if not first:
                                    further_sums(1 - b, s - 1)
                                own_base, own_more = window_parts_of(s, pe)
                                with pe.If(own_more > 0):
                                    seen = before(pe, s)
                                    with pe.Fori(0, own_more) as w:
                                        hold(pe, relx_ready, seen + w + 1)
                                        for k in range(K):
                                            last = pe.matmul(ps_dst[:, k, :], relxb[:, k:k + 1].to_broadcast([P, P]),
                                                             identb[:, :], start=True, stop=True)
                                        last.then_inc(dstx_spread, 1)
                                        hold(pe, hotx_ready, seen + w + 1)
                                        hold(pe, win_x, (seen + w + 1) * 16)
                                        for k in range(K):
                                            last = pe.matmul(ps_pre[:, b, k, :], hot_t[:, b, k, :], b_win[:, b, :],
                                                             start=False, stop=False, skip_group_check=True)
                                        last.then_inc(prex_done, 1)
                                pe.drain()
                            for k in range(K):
                                pe.wait_ge(slot_done[b][k], ROUND + 16 * i + 16)
                                last = pe.matmul(ps_pre[:, b, k, :], ident[:, :], a_rows[:, b, k, :], start=False,
                                                 stop=(k == K - 1), skip_group_check=True)
                                if k == 0 and not first:
                                    last.then_inc(seg_done, 1)
                            last.then_inc(pre_done, 1)
                            spread(1 - b, s + 1)
                    sum_by_node(1, SUPERS - 1)
                    further_sums(1, SUPERS - 1)

                @block.scalar
                def _(act):
                    act.wait_ge(ones_ready, 1)
                    for i in first_then_loop(act, HALF):
                        for b in range(2):
                            s = 2 * i + b
                            hold(act, seg_done, s - 1)
                            hold(act, pre_done, s + 1)
                            nc.scalar.activation(act_rows[:, b, :, 0:F], ps_pre[:, b, :, :], ACT.Relu).then_inc(act_ready, 1)
        end_stage()

        with ExitStack() as ph:
            c5 = ExitStack()
            h_st = sb(c5, "h_st5", [P, 2, JG, F])
            acc_st = sb(c5, "acc_st5", [F + 1, 2, GN])
            ha_t = sb(c5, "ha_t", [P, 2, GN])
            gates = sb(c5, "gates", [P, 2, JG, 4 * F])
            rz = sb(c5, "rz", [P, 2, JG, 2 * F])
            cand = sb(c5, "cand", [P, 2, JG, F])
            new = sb(c5, "new", [P, 2, JG, F])
            mix = sb(c5, "mix", [P, 2, JG, F])
            cnt_j = sb(c5, "cnt_j", [J, P])
            cnt_n = sb(c5, "cnt_n", [P, J])
            ps_ha = psum(c5, "ps_ha", [P, 2, GN])
            ps_g = psum(c5, "ps_g", [P, 2, JG, 4 * F])
            ps_c = psum(c5, "ps_c", [P, 512])
            cnt_out, cnt_back, cnt_turned, cnt_copied, cnt_max = (
                sem(f"n2_{n}") for n in ("cnt_out", "cnt_back", "cnt_turned", "cnt_copied", "cnt_max"))
            acc_staged, staged, ha_done, ha_copied, g_done, g_biased, rz_ready, rh, pre_n, n_ready, d1, d2, d3, x_done = (
                sem(f"n2_{n}") for n in ("acc_staged", "staged", "ha_done", "ha_copied", "g_done", "g_biased", "rz_ready", "rh",
                                         "pre_n", "n_ready", "d1", "d2", "d3", "x_done"))
            with nc.Block() as block:
                @block.sync
                def _(sp):
                    sp.dma_start(cnt_tab.rearrange("(a j) p -> a (j p)", a=1), acc_t[F:F + 1, :]).then_inc(cnt_out, 16)
                    sp.wait_ge(cnt_out, 16)
                    sp.dma_start(cnt_j[:, :], cnt_tab).then_inc(cnt_back, 16)
                    sp.wait_ge(cnt_back, 16)

                @block.gpsimd
                def _(pool):
                    def blend(b, g):
                        cols = bass.ds(g * JG, JG)
                        pool.wait_ge(n_ready, g + 1)
                        need(pool, x_done, g - 1)
                        pool.tensor_tensor(mix[:, b, :, :], h_st[:, b, :, :], new[:, b, :, :], ALU.subtract).then_inc(d1, 1)
                        pool.wait_ge(d1, g + 1)
                        pool.tensor_tensor(mix[:, b, :, :], mix[:, b, :, :], rz[:, b, :, F:2 * F], ALU.mult).then_inc(d2, 1)

                    for i in first_then_loop(pool, GROUPS // 2):
                        for b in range(2):
                            g = 2 * i + b
                            hold(pool, ha_done, g - 1)
                            hold(pool, d1, g - 1)
                            pool.tensor_copy(h_st[:, b, :, :], h_nm[:, bass.ds(g * JG, JG), :]).then_inc(staged, 1)
                            if not (isinstance(g, int) and g == 0):
                                blend(1 - b, g - 1)
                    blend(1, GROUPS - 1)

                @block.tensor
                def _(pe):
                    pe.wait_ge(cnt_back, 16)
                    pe.transpose(ps_c[:, 0:J], cnt_j[:, :], ident[0:J, 0:J]).then_inc(cnt_turned, 1)
                    def gate_sums(b, g):
                        pe.wait_ge(ha_copied, g + 1)
                        need(pe, g_biased, g - 1)
                        for q in range(JG):
                            last = pe.matmul(ps_g[:, b, q, :], ha_t[:, b, q * P:(q + 1) * P], wg_sb[:, :],
                                             start=True, stop=True)
                        last.then_inc(g_done, 1)

                    for i in first_then_loop(pe, GROUPS // 2):
                        for b in range(2):
                            g = 2 * i + b
                            pe.wait_ge(staged, g + 1)
                            hold(pe, ha_copied, g - 1)
                            for q in range(JG):
                                pe.transpose(ps_ha[0:F, b, q * P:(q + 1) * P], h_st[:, b, q, :], ident[:, :])
                            pe.wait_ge(acc_staged, g + 1)
                            pe.matmul(ps_ha[F:2 * F, b, :], w2_sb[:, :], acc_st[:, b, :],
                                      start=True, stop=True).then_inc(ha_done, 1)
                            if not (isinstance(g, int) and g == 0):
                                gate_sums(1 - b, g - 1)
                    gate_sums(1, GROUPS - 1)

                @block.scalar
                def _(act):
                    def gate_functions(b, g):
                        act.wait_ge(g_biased, g + 1)
                        need(act, d2, g - 1)
                        nc.scalar.activation(rz[:, b, :, :], gates[:, b, :, 0:2 * F], ACT.Sigmoid).then_inc(rz_ready, 1)
                        act.wait_ge(pre_n, g + 1)
                        need(act, d3, g - 1)
                        nc.scalar.activation(new[:, b, :, :], cand[:, b, :, :], ACT.Tanh).then_inc(n_ready, 1)

                    act.wait_ge(cnt_turned, 1)
                    nc.scalar.activation(cnt_n[:, :], ps_c[:, 0:J], ACT.Copy).then_inc(cnt_copied, 1)
                    for i in first_then_loop(act, GROUPS // 2):
                        for b in range(2):
                            g = 2 * i + b
                            hold(act, ha_done, g - 1)
                            nc.scalar.activation(acc_st[:, b, :], acc_t[0:F + 1, bass.ds(g * GN, GN)],
                                                 ACT.Copy).then_inc(acc_staged, 1)
                            act.wait_ge(ha_done, g + 1)
                            need(act, g_done, g - 1)
                            nc.scalar.activation(ha_t[:, b, :], ps_ha[:, b, :], ACT.Copy).then_inc(ha_copied, 1)
                            if not (isinstance(g, int) and g == 0):
                                gate_functions(1 - b, g - 1)
                    gate_functions(1, GROUPS - 1)

                @block.vector
                def _(dve):
                    dve.wait_ge(cnt_copied, 1)
                    dve.tensor_scalar(rcnt[:, :], cnt_n[:, :], 1.0, None, ALU.max).then_inc(cnt_max, 1)
                    dve.wait_ge(cnt_max, 1)
                    dve.reciprocal(rcnt[:, :], rcnt[:, :]).then_inc(cnt_max, 1)

                    def finish(b, g):
                        cols = bass.ds(g * JG, JG)
                        dve.wait_ge(d2, g + 1)
                        dve.tensor_tensor(mix[:, b, :, :], mix[:, b, :, :], new[:, b, :, :], ALU.add).then_inc(d3, 1)
                        dve.wait_ge(d3, g + 1)
                        dve.tensor_tensor(x_nm[:, cols, :], x_nm[:, cols, :], mix[:, b, :, :], ALU.add).then_inc(x_done, 1)

                    for i in first_then_loop(dve, GROUPS // 2):
                        for b in range(2):
                            g = 2 * i + b
                            dve.wait_ge(g_done, g + 1)
                            need(dve, pre_n, g - 1)
                            need(dve, rz_ready, g - 1)
                            dve.tensor_tensor(gates[:, b, :, :], ps_g[:, b, :, :],
                                              bg_sb[:, None, :].to_broadcast([P, JG, 4 * F]), ALU.add).then_inc(g_biased, 1)
                            if not (isinstance(g, int) and g == 0):
                                finish(1 - b, g - 1)
                            dve.wait_ge(rz_ready, g + 1)
                            need(dve, n_ready, g - 1)
                            dve.tensor_tensor(cand[:, b, :, :], rz[:, b, :, 0:F], gates[:, b, :, 3 * F:4 * F],
                                              ALU.mult).then_inc(rh, 1)
                            dve.wait_ge(rh, g + 1)
                            dve.tensor_tensor(cand[:, b, :, :], cand[:, b, :, :], gates[:, b, :, 2 * F:3 * F],
                                              ALU.add).then_inc(pre_n, 1)
                    finish(1, GROUPS - 1)
                    dve.wait_ge(x_done, GROUPS)
            c5.close()

            norm = Norm(ph, 2, smalls_before=9 * CHUNKS)
            with nc.Block() as block:
                @block.vector
                def _(dve):
                    norm.vector(dve)

                @block.scalar
                def _(act):
                    norm.activation(act)

                @block.sync
                def _(sp):
                    norm.store(sp, h2_tab, 1)

        def edge_sums(layer, table):
            with ExitStack() as ph:
                idx = sb(ph, f"idx{layer}", [P, 2, K], I32)
                rows_of = sb(ph, f"h_rows{layer}", [P, 2, K, F])
                rel = sb(ph, f"rel{layer}", [P, K])
                hot = sb(ph, f"hot{layer}", [P, 2, K, P])
                ps_seg = psum(ph, f"ps_seg{layer}", [P, 2, 4, P])
                idx_in = [sem(f"l{layer}_idx_in{b}") for b in range(2)]
                cleared, rel_ready, hot_ready, seg_main, seg_done, acc_done, segx_hot, segx_done = (
                    sem(f"l{layer}_{n}") for n in ("cleared", "rel_ready", "hot_ready", "seg_main", "seg_done",
                                                   "acc_done", "segx_hot", "segx_done"))
                landed = ROUND * layer
                with nc.Block() as block:
                    @block.sync
                    def _(sp):
                        for i in first_then_loop(sp, HALF):
                            for b in range(2):
                                s = 2 * i + b
                                hold(sp, slot_done[b][K - 1], landed + 16 * i)
                                sp.dma_start(idx[:, b, :], src_steps[bass.ds(s, 1), :, :].rearrange("s p k -> p (s k)")
                                             ).then_inc(idx_in[b], 16)

                    @block.gpsimd
                    def _(pool):
                        gather_slots(pool, idx_in, idx, table, rows_of, seg_done)

                    @block.vector
                    def _(dve):
                        dve.memset(acc_t[0:F, :], 0.0).then_inc(cleared, 1)
                        dve.wait_ge(cleared, 1)
                        for i in first_then_loop(dve, HALF):
                            for b in range(2):
                                s = 2 * i + b
                                base, more = window_parts(i, b, dve)
                                hold(dve, hot_ready, s)
                                dve.tensor_scalar(rel[:, :], dstf[:, bass.ds(s * K, K)], base_all[:, bass.ds(s, 1)],
                                                  None, ALU.subtract).then_inc(rel_ready, 1)
                                hold(dve, seg_done, s - 1)
                                hold(dve, rel_ready, s + 1)
                                dve.tensor_tensor(hot[:, b, :, :], iotab[:, None, :].to_broadcast([P, K, P]),
                                                  rel[:, :, None].to_broadcast([P, K, P]), ALU.is_equal).then_inc(hot_ready, 1)
                                cols = acc_t[0:F, bass.ds(base, P)]
                                hold(dve, acc_done, s)
                                hold(dve, seg_main, s + 1)
                                dve.tensor_tensor(cols, cols, ps_seg[0:F, b, 0, :], ALU.add).then_inc(acc_done, 1)
                                with dve.If(more > 0):
                                    seen = before(dve, s)
                                    hold(dve, acc_done, s + 1)
                                    hold(dve, hot_ready, s + 1)
                                    with dve.Fori(0, more) as w:
                                        dve.tensor_scalar(rel[:, :], rel[:, :], -float(P), None, ALU.add)
                                        dve.drain()
                                        dve.tensor_tensor(hot[:, b, :, :], iotab[:, None, :].to_broadcast([P, K, P]),
                                                          rel[:, :, None].to_broadcast([P, K, P]),
                                                          ALU.is_equal).then_inc(segx_hot, 1)
                                        hold(dve, segx_done, seen + w + 1)
                                        far = acc_t[0:F, bass.ds(further(dve, base, w), P)]
                                        dve.tensor_tensor(far, far, ps_seg[0:F, b, 0, :], ALU.add)
                                        dve.drain()

                    @block.tensor
                    def _(pe):
                        for i in first_then_loop(pe, HALF):
                            for b in range(2):
                                s = 2 * i + b
                                word = pe.value_load(meta[0:1, bass.ds(s, 1)], min_val=0, max_val=BASE_MAX * PACK + PACK - 1)
                                more = word % PACK
                                pe.wait_ge(hot_ready, s + 1)
                                need(pe, acc_done, s - 1)
                                for k in range(K):
                                    pe.wait_ge(slot_done[b][k], landed + 16 * i + 16)
                                    last = pe.matmul(ps_seg[0:F, b, 0, :], rows_of[:, b, k, :], hot[:, b, k, :],
                                                     start=(k == 0), stop=(k == K - 1))
                                last.then_inc(seg_main, 1)
                                with pe.If(more > 0):
                                    seen = before(pe, s)
                                    with pe.Fori(0, more) as w:
                                        hold(pe, segx_hot, seen + w + 1)
                                        for k in range(K):
                                            last = pe.matmul(ps_seg[0:F, b, 0, :], rows_of[:, b, k, :], hot[:, b, k, :],
                                                             start=(k == 0), stop=(k == K - 1))
                                        last.then_inc(segx_done, 1)
                                pe.drain().then_inc(seg_done, 1)
        end_stage()

        edge_sums(2, h2_tab)
        end_stage()
        with ExitStack() as ph:
            c6 = ExitStack()
            h_st = sb(c6, "h_st6", [P, 2, JG, F])
            z_t = sb(c6, "z_t", [F, 2, GN])
            hid = sb(c6, "hid", [HID, 2, GN])
            upd = sb(c6, "upd6", [P, 2, JG, F])
            ps_h = psum(c6, "ps_h6", [F, 2, GN])
            ps_hid = psum(c6, "ps_hid", [HID, 2, GN])
            ps_out = psum(c6, "ps_out6", [P, 2, 8, F])
            staged, turned, z_ready, hid_done, hid_ready, out_ready, upd_ready, x_done = (
                sem(f"n3_{n}") for n in ("staged", "turned", "z_ready", "hid_done", "hid_ready", "out_ready",
                                         "upd_ready", "x_done"))
            with nc.Block() as block:
                @block.gpsimd
                def _(pool):
                    for i in first_then_loop(pool, GROUPS // 2):
                        for b in range(2):
                            g = 2 * i + b
                            hold(pool, turned, g - 1)
                            pool.tensor_copy(h_st[:, b, :, :], h_nm[:, bass.ds(g * JG, JG), :]).then_inc(staged, 1)

                @block.tensor
                def _(pe):
                    def turn(b, g):
                        pe.wait_ge(staged, g + 1)
                        hold(pe, z_ready, g - 1)
                        for q in range(JG):
                            last = pe.transpose(ps_h[:, b, q * P:(q + 1) * P], h_st[:, b, q, :], ident[:, :])
                        last.then_inc(turned, 1)

                    def mlp(b, g):
                        pe.wait_ge(z_ready, g + 1)
                        need(pe, hid_ready, g - 1)
                        pe.matmul(ps_hid[:, b, :], w21_sb[:, :], z_t[:, b, :], start=True, stop=True).then_inc(hid_done, 1)
                        pe.wait_ge(hid_ready, g + 1)
                        need(pe, upd_ready, g - 1)
                        for q in range(JG):
                            last = pe.matmul(ps_out[:, b, q, :], hid[:, b, q * P:(q + 1) * P], w22_sb[:, :],
                                             start=True, stop=True)
                        last.then_inc(out_ready, 1)

                    for i in first_then_loop(pe, GROUPS // 2):
                        for b in range(2):
                            g = 2 * i + b
                            turn(b, g)
                            if not (isinstance(g, int) and g == 0):
                                mlp(1 - b, g - 1)
                    mlp(1, GROUPS - 1)

                @block.scalar
                def _(act):
                    for i in first_then_loop(act, GROUPS // 2):
                        for b in range(2):
                            g = 2 * i + b
                            act.wait_ge(hid_done, g + 1)
                            need(act, out_ready, g - 1)
                            nc.scalar.activation(hid[:, b, :], ps_hid[:, b, :], ACT.Relu,
                                                 bias=b21_sb[:, 0:1]).then_inc(hid_ready, 1)

                @block.vector
                def _(dve):
                    def finish(b, g):
                        cols = bass.ds(g * JG, JG)
                        dve.wait_ge(out_ready, g + 1)
                        dve.tensor_tensor(upd[:, b, :, :], ps_out[:, b, 0:JG, :],
                                          b22_sb[:, None, :].to_broadcast([P, JG, F]), ALU.add).then_inc(upd_ready, 1)
                        dve.wait_ge(upd_ready, g + 1)
                        dve.tensor_tensor(x_nm[:, cols, :], x_nm[:, cols, :], upd[:, b, :, :], ALU.add).then_inc(x_done, 1)

                    for i in first_then_loop(dve, GROUPS // 2):
                        for b in range(2):
                            g = 2 * i + b
                            dve.wait_ge(turned, g + 1)
                            need(dve, hid_done, g - 1)
                            dve.scalar_tensor_tensor(out=z_t[:, b, :], in0=ps_h[:, b, :], scalar=eps1[0:F, 0:1],
                                                     in1=acc_t[0:F, bass.ds(g * GN, GN)], op0=ALU.mult,
                                                     op1=ALU.add).then_inc(z_ready, 1)
                            if not (isinstance(g, int) and g == 0):
                                finish(1 - b, g - 1)
                    finish(1, GROUPS - 1)
                    dve.wait_ge(x_done, GROUPS)
            c6.close()

            norm = Norm(ph, 3, smalls_before=13 * CHUNKS)
            with nc.Block() as block:
                @block.vector
                def _(dve):
                    norm.vector(dve)

                @block.scalar
                def _(act):
                    norm.activation(act)

                @block.sync
                def _(sp):
                    norm.store(sp, h3_tab, 2)
        end_stage()

        edge_sums(3, h3_tab)
        end_stage()
        with ExitStack() as ph:
            h_st = sb(ph, "h_st7", [P, 2, JG, F])
            acc_st = sb(ph, "acc_st", [F, 2, GN])
            h_t = sb(ph, "h_t7", [F + 1, 2, GN])
            lin = sb(ph, "lin", [P, 2, JG, F])
            ps_h = psum(ph, "ps_h7", [F, 2, GN])
            ps_l = psum(ph, "ps_l", [P, 2, 8, F])
            ps_r = psum(ph, "ps_r", [P, 2, 8, F])
            ones_set, staged, acc_staged, turned, h_t_ready, l_done, r_done, meaned, summed, x_done, stored = (
                sem(f"n4_{n}") for n in ("ones_set", "staged", "acc_staged", "turned", "h_t_ready", "l_done", "r_done",
                                         "meaned", "summed", "x_done", "stored"))
            with nc.Block() as block:
                @block.gpsimd
                def _(pool):
                    for i in first_then_loop(pool, GROUPS // 2):
                        for b in range(2):
                            g = 2 * i + b
                            hold(pool, turned, g - 1)
                            pool.tensor_copy(h_st[:, b, :, :], h_nm[:, bass.ds(g * JG, JG), :]).then_inc(staged, 1)
                            hold(pool, l_done, g - 1)
                            pool.tensor_copy(acc_st[:, b, :], acc_t[0:F, bass.ds(g * GN, GN)]).then_inc(acc_staged, 1)

                @block.tensor
                def _(pe):
                    pe.wait_ge(ones_set, 1)
                    for i in first_then_loop(pe, GROUPS // 2):
                        for b in range(2):
                            g = 2 * i + b
                            pe.wait_ge(staged, g + 1)
                            hold(pe, h_t_ready, g - 1)
                            for q in range(JG):
                                last = pe.transpose(ps_h[:, b, q * P:(q + 1) * P], h_st[:, b, q, :], ident[:, :])
                            last.then_inc(turned, 1)
                            pe.wait_ge(acc_staged, g + 1)
                            need(pe, meaned, g - 1)
                            for q in range(JG):
                                last = pe.matmul(ps_l[:, b, q, :], acc_st[:, b, q * P:(q + 1) * P], wl3_sb[:, :],
                                                 start=True, stop=True)
                            last.then_inc(l_done, 1)
                            pe.wait_ge(h_t_ready, g + 1)
                            need(pe, summed, g - 1)
                            for q in range(JG):
                                last = pe.matmul(ps_r[:, b, q, :], h_t[:, b, q * P:(q + 1) * P], wr3_sb[:, :],
                                                 start=True, stop=True)
                            last.then_inc(r_done, 1)

                @block.scalar
                def _(act):
                    for i in first_then_loop(act, GROUPS // 2):
                        for b in range(2):
                            g = 2 * i + b
                            act.wait_ge(turned, g + 1)
                            need(act, r_done, g - 1)
                            nc.scalar.activation(h_t[0:F, b, :], ps_h[:, b, :], ACT.Copy).then_inc(h_t_ready, 1)

                @block.vector
                def _(dve):
                    dve.memset(h_t[F:F + 1, :, :], 1.0).then_inc(ones_set, 1)
                    for i in first_then_loop(dve, GROUPS // 2):
                        for b in range(2):
                            g = 2 * i + b
                            cols = bass.ds(g * JG, JG)
                            dve.wait_ge(l_done, g + 1)
                            need(dve, x_done, g - 1)
                            dve.tensor_tensor(lin[:, b, :, :], ps_l[:, b, 0:JG, :],
                                              rcnt[:, cols, None].to_broadcast([P, JG, F]), ALU.mult).then_inc(meaned, 1)
                            dve.wait_ge(meaned, g + 1)
                            dve.wait_ge(r_done, g + 1)
                            dve.tensor_tensor(lin[:, b, :, :], lin[:, b, :, :], ps_r[:, b, 0:JG, :],
                                              ALU.add).then_inc(summed, 1)
                            dve.wait_ge(summed, g + 1)
                            dve.scalar_tensor_tensor(out=x_nm[:, cols, :], in0=lin[:, b, :, :], scalar=0.0,
                                                     in1=x_nm[:, cols, :], op0=ALU.max, op1=ALU.add).then_inc(x_done, 1)

                @block.sync
                def _(sp):
                    for c in range(2):
                        cc = slice(c * (J // 2), (c + 1) * (J // 2))
                        sp.wait_ge(x_done, (c + 1) * GROUPS // 2)
                        sp.dma_start(by_node(out)[:, cc, :], x_nm[:, cc, :]).then_inc(stored, 16)
                    sp.wait_ge(stored, 32)


def _laid_out(v, np):
    def f32(shape):
        return np.zeros(shape, np.float32)

    x = f32((NP, F))
    x[:N_NODES] = v["x"]
    ids = {}
    for name in ("src", "dst"):
        a = np.full(EP, PAD_NODE, np.int32)
        a[:N_EDGES] = v[name]
        ids[name] = a.reshape(TILES, P)
    edge_t = f32((EDGE_F + 1, EP))
    edge_t[:EDGE_F, :N_EDGES] = v["edge_attr_32"].T
    edge_t[EDGE_F] = 1.0

    def twice(w):
        a = f32((2 * F, 2 * F))
        a[:F, :F] = w
        a[F:, F:] = w
        return a

    w1, wih, whh = v["L1_gnn_W1"], v["L1_gnn_w_ih"], v["L1_gnn_w_hh"]
    gate = f32((2 * F, 4 * F))
    gate[:F, :2 * F] = whh[:2 * F].T
    gate[:F, 3 * F:] = whh[2 * F:].T
    gate[F:, :3 * F] = wih.T
    return {
        "x_in": x,
        "src_steps": ids["src"].reshape(SUPERS, K, P).transpose(0, 2, 1),
        "src_cols": ids["src"].T,
        "dst_cols": ids["dst"].T,
        "edge_t": edge_t,
        "w0bd": twice(v["L0_gnn_W"]),
        "w1ab": np.concatenate([twice(w1[:, :F].T), twice(w1[:, F:2 * F].T)], 1),
        "w1c": np.concatenate([w1[:, 2 * F:].T, v["L1_gnn_b1"][None]], 0),
        "w2b": np.concatenate([v["L1_gnn_W2"].T, v["L1_gnn_b2"][None]], 0),
        "wgate": gate,
        "bih": v["L1_gnn_b_ih"][None],
        "bhh": v["L1_gnn_b_hh"][None],
        "w21": v["L2_gnn_W1"],
        "b21": v["L2_gnn_b1"][:, None],
        "w22": v["L2_gnn_W2"],
        "b22": v["L2_gnn_b2"][None],
        "eps_in": v["L2_gnn_eps"][None],
        "wl3": v["L3_gnn_W_l"].T,
        "wr3b": np.concatenate([v["L3_gnn_W_r"].T, v["L3_gnn_b_l"][None]], 0),
    }


def kernel(**inputs):
    import numpy as np
    import concourse.bacc as bacc
    from concourse.bass_utils import run_bass_kernel_spmd

    arrays = {n: np.ascontiguousarray(a) for n, a in
              _laid_out({n: np.asarray(a) for n, a in inputs.items()}, np).items()}
    nc = bacc.Bacc("TRN2", target_bir_lowering=False, num_devices=1)
    aps = {n: nc.dram_tensor(n, a.shape, mybir.dt.from_np(a.dtype), kind="ExternalInput").ap()
           for n, a in arrays.items()}
    aps["out"] = nc.dram_tensor("out", (NP, F), F32, kind="ExternalOutput").ap()
    gnn_kernel(nc, **aps)
    r = run_bass_kernel_spmd(nc, [arrays], core_ids=[0])
    return r.results[0]["out"][:N_NODES]
```
